# Optimizing a Trainium2 kernel written in Bass

```python
import numpy as np
import jax
import jax.numpy as jnp

def _softmax(x, axis=-1):
    return jax.nn.softmax(x, axis=axis)

def _gelu(x):
    return jax.nn.gelu(x, approximate=True)

def _silu(x):
    return jax.nn.silu(x)

def _sigmoid(x):
    return jax.nn.sigmoid(x)

def _layernorm(x, axis=-1, eps=1e-05):
    m = jnp.mean(x, axis=axis, keepdims=True)
    v = jnp.var(x, axis=axis, keepdims=True)
    return (x - m) / jnp.sqrt(v + eps)

def _scatter_add(tgt, idx, src, axis=0):
    return tgt.at[idx].add(src)

def _segment_sum(src, seg, n):
    return jax.ops.segment_sum(src, seg, n)
kernel_name = 'mk_dlrm_tower_d1_rec_r8_e23ac3'

def setup_inputs(seed: int=0):
    np.random.seed(seed)
    _w = jnp.asarray

    def _rec_inputs():
        import jax
        import jax.numpy as jnp
        _tk = jax.random.key(seed)
        ids = jnp.stack([jax.random.randint(jax.random.fold_in(_tk, 200 + f), (512,), 0, v, jnp.int32) for f, v in enumerate([12500, 1250, 12500, 1250, 12500, 12500, 125000, 12500, 12500, 1000, 1250, 1000, 12500, 1000, 12500, 12500, 1000, 1000, 1250, 1000, 1000, 1000, 1000, 1000, 1000, 1000])], axis=1)
        tbl_0 = 0.05 * jax.random.normal(jax.random.fold_in(_tk, 500 + 0), (12500, 128), jnp.float32)
        tbl_1 = 0.05 * jax.random.normal(jax.random.fold_in(_tk, 500 + 1), (1250, 128), jnp.float32)
        tbl_2 = 0.05 * jax.random.normal(jax.random.fold_in(_tk, 500 + 2), (12500, 128), jnp.float32)
        tbl_3 = 0.05 * jax.random.normal(jax.random.fold_in(_tk, 500 + 3), (1250, 128), jnp.float32)
        tbl_4 = 0.05 * jax.random.normal(jax.random.fold_in(_tk, 500 + 4), (12500, 128), jnp.float32)
        tbl_5 = 0.05 * jax.random.normal(jax.random.fold_in(_tk, 500 + 5), (12500, 128), jnp.float32)
        tbl_6 = 0.05 * jax.random.normal(jax.random.fold_in(_tk, 500 + 6), (125000, 128), jnp.float32)
        tbl_7 = 0.05 * jax.random.normal(jax.random.fold_in(_tk, 500 + 7), (12500, 128), jnp.float32)
        tbl_8 = 0.05 * jax.random.normal(jax.random.fold_in(_tk, 500 + 8), (12500, 128), jnp.float32)
        tbl_9 = 0.05 * jax.random.normal(jax.random.fold_in(_tk, 500 + 9), (1000, 128), jnp.float32)
        tbl_10 = 0.05 * jax.random.normal(jax.random.fold_in(_tk, 500 + 10), (1250, 128), jnp.float32)
        tbl_11 = 0.05 * jax.random.normal(jax.random.fold_in(_tk, 500 + 11), (1000, 128), jnp.float32)
        tbl_12 = 0.05 * jax.random.normal(jax.random.fold_in(_tk, 500 + 12), (12500, 128), jnp.float32)
        tbl_13 = 0.05 * jax.random.normal(jax.random.fold_in(_tk, 500 + 13), (1000, 128), jnp.float32)
        tbl_14 = 0.05 * jax.random.normal(jax.random.fold_in(_tk, 500 + 14), (12500, 128), jnp.float32)
        tbl_15 = 0.05 * jax.random.normal(jax.random.fold_in(_tk, 500 + 15), (12500, 128), jnp.float32)
        tbl_16 = 0.05 * jax.random.normal(jax.random.fold_in(_tk, 500 + 16), (1000, 128), jnp.float32)
        tbl_17 = 0.05 * jax.random.normal(jax.random.fold_in(_tk, 500 + 17), (1000, 128), jnp.float32)
        tbl_18 = 0.05 * jax.random.normal(jax.random.fold_in(_tk, 500 + 18), (1250, 128), jnp.float32)
        tbl_19 = 0.05 * jax.random.normal(jax.random.fold_in(_tk, 500 + 19), (1000, 128), jnp.float32)
        tbl_20 = 0.05 * jax.random.normal(jax.random.fold_in(_tk, 500 + 20), (1000, 128), jnp.float32)
        tbl_21 = 0.05 * jax.random.normal(jax.random.fold_in(_tk, 500 + 21), (1000, 128), jnp.float32)
        tbl_22 = 0.05 * jax.random.normal(jax.random.fold_in(_tk, 500 + 22), (1000, 128), jnp.float32)
        tbl_23 = 0.05 * jax.random.normal(jax.random.fold_in(_tk, 500 + 23), (1000, 128), jnp.float32)
        tbl_24 = 0.05 * jax.random.normal(jax.random.fold_in(_tk, 500 + 24), (1000, 128), jnp.float32)
        tbl_25 = 0.05 * jax.random.normal(jax.random.fold_in(_tk, 500 + 25), (1000, 128), jnp.float32)
        _rk = jax.random.fold_in(_tk, 7)
        r_dense_features = -0.000520686 + 1.00062 * jax.random.normal(jax.random.fold_in(_rk, 101), (512, 128), jnp.float32)
        W_top1 = 0.0405887 * jax.random.normal(jax.random.fold_in(_tk, 801), (607, 512), jnp.float32)
        W_top2 = 0.0441942 * jax.random.normal(jax.random.fold_in(_tk, 802), (512, 256), jnp.float32)
        W_top3 = 0.0625 * jax.random.normal(jax.random.fold_in(_tk, 803), (256, 1), jnp.float32)
        b_top1 = jnp.zeros((512,), jnp.float32)
        b_top2 = jnp.zeros((256,), jnp.float32)
        return (r_dense_features, ids, tbl_0, tbl_1, tbl_2, tbl_3, tbl_4, tbl_5, tbl_6, tbl_7, tbl_8, tbl_9, tbl_10, tbl_11, tbl_12, tbl_13, tbl_14, tbl_15, tbl_16, tbl_17, tbl_18, tbl_19, tbl_20, tbl_21, tbl_22, tbl_23, tbl_24, tbl_25, W_top1, b_top1, W_top2, b_top2, W_top3)
    r_dense_features, ids, tbl_0, tbl_1, tbl_2, tbl_3, tbl_4, tbl_5, tbl_6, tbl_7, tbl_8, tbl_9, tbl_10, tbl_11, tbl_12, tbl_13, tbl_14, tbl_15, tbl_16, tbl_17, tbl_18, tbl_19, tbl_20, tbl_21, tbl_22, tbl_23, tbl_24, tbl_25, W_top1, b_top1, W_top2, b_top2, W_top3 = _rec_inputs()

    def _L0_rec_setup():
        import jax, jax.numpy as jnp
        import numpy as np
        F = 26
        key = jax.random.key(seed)
        k1, k2 = jax.random.split(key)
        B, D = (2048, 128)
        dense_features = jax.random.normal(k1, (B, D), dtype=jnp.float32)
        sparse_features = jax.random.normal(k2, (B, F, D), dtype=jnp.float32)
        return {'dense_features': dense_features, 'sparse_features': sparse_features}
    _L0_rec_all = _L0_rec_setup()
    _L0_rec_in = {k: v for k, v in _L0_rec_all.items() if k in ()}
    del _L0_rec_all
    return {'r_dense_features': r_dense_features, 'ids': ids, 'tbl_0': tbl_0, 'tbl_1': tbl_1, 'tbl_2': tbl_2, 'tbl_3': tbl_3, 'tbl_4': tbl_4, 'tbl_5': tbl_5, 'tbl_6': tbl_6, 'tbl_7': tbl_7, 'tbl_8': tbl_8, 'tbl_9': tbl_9, 'tbl_10': tbl_10, 'tbl_11': tbl_11, 'tbl_12': tbl_12, 'tbl_13': tbl_13, 'tbl_14': tbl_14, 'tbl_15': tbl_15, 'tbl_16': tbl_16, 'tbl_17': tbl_17, 'tbl_18': tbl_18, 'tbl_19': tbl_19, 'tbl_20': tbl_20, 'tbl_21': tbl_21, 'tbl_22': tbl_22, 'tbl_23': tbl_23, 'tbl_24': tbl_24, 'tbl_25': tbl_25, 'W_top1': W_top1, 'b_top1': b_top1, 'W_top2': W_top2, 'b_top2': b_top2, 'W_top3': W_top3}

def reference(r_dense_features, ids, tbl_0, tbl_1, tbl_2, tbl_3, tbl_4, tbl_5, tbl_6, tbl_7, tbl_8, tbl_9, tbl_10, tbl_11, tbl_12, tbl_13, tbl_14, tbl_15, tbl_16, tbl_17, tbl_18, tbl_19, tbl_20, tbl_21, tbl_22, tbl_23, tbl_24, tbl_25, W_top1, b_top1, W_top2, b_top2, W_top3):
    import jax
    import jax.numpy as jnp

    def _L0_rec_ref(dense_features, sparse_features):
        import jax, jax.numpy as jnp
        import numpy as np
        F = 26
        B, D = dense_features.shape
        combined = jnp.concatenate((dense_features[:, None, :], sparse_features), axis=1)
        interactions = jnp.einsum('bfd,bgd->bfg', combined, combined)
        iu, ju = jnp.triu_indices(F + 1, k=1)
        interactions_flat = interactions[:, iu, ju]
        return jnp.concatenate((dense_features, interactions_flat), axis=1)
    e = jnp.stack([tbl_0[ids[:, 0]], tbl_1[ids[:, 1]], tbl_2[ids[:, 2]], tbl_3[ids[:, 3]], tbl_4[ids[:, 4]], tbl_5[ids[:, 5]], tbl_6[ids[:, 6]], tbl_7[ids[:, 7]], tbl_8[ids[:, 8]], tbl_9[ids[:, 9]], tbl_10[ids[:, 10]], tbl_11[ids[:, 11]], tbl_12[ids[:, 12]], tbl_13[ids[:, 13]], tbl_14[ids[:, 14]], tbl_15[ids[:, 15]], tbl_16[ids[:, 16]], tbl_17[ids[:, 17]], tbl_18[ids[:, 18]], tbl_19[ids[:, 19]], tbl_20[ids[:, 20]], tbl_21[ids[:, 21]], tbl_22[ids[:, 22]], tbl_23[ids[:, 23]], tbl_24[ids[:, 24]], tbl_25[ids[:, 25]]], axis=1)
    z = _L0_rec_ref(r_dense_features, e)
    z = z.reshape(z.shape[0], -1)
    h = jnp.concatenate([z, r_dense_features], axis=1)
    h = jnp.maximum(h @ W_top1 + b_top1, 0.0)
    h = jnp.maximum(h @ W_top2 + b_top2, 0.0)
    y = h @ W_top3
    return y

_drawn_inputs = setup_inputs


def setup_inputs(seed=0):
    import zlib

    import numpy as np

    out = dict(_drawn_inputs(seed))
    spreads = {'b_top1': (0.0, 0.1), 'b_top2': (0.0, 0.1)}
    factors = {}
    for name, (base, spread) in spreads.items():
        noise = np.random.default_rng([zlib.crc32(name.encode()), seed]).standard_normal(out[name].shape)
        drawn = base * np.exp(spread * noise) if base else spread * noise
        out[name] = jnp.asarray(drawn.astype(out[name].dtype))
    for name, factor in factors.items():
        out[name] = (out[name] * factor).astype(out[name].dtype)
    return out
```

```python
from contextlib import ExitStack

import numpy as np

import concourse.bass as bass
from concourse import mybir

F32 = mybir.dt.float32
F32R = mybir.dt.float32r
I32 = mybir.dt.int32
ALU = mybir.AluOpType
ACT = mybir.ActivationFunctionType

P = 128
BATCH = 512
TABLES = 26
SLOTS = TABLES + 1
D = 128
TILES = BATCH // P
N1, N2 = 512, 256
N1_BLOCKS, N2_BLOCKS = N1 // P, N2 // P

ONEHOT_TABLES = [11, 13, 16, 17, 19, 20, 21, 22, 23, 24][-8:]
ONEHOT_ROWS = 1000
ONEHOT_CHUNKS = 8
ONEHOT_PARTS = ONEHOT_ROWS // ONEHOT_CHUNKS
GATHER_TABLES = [t for t in range(TABLES) if t not in ONEHOT_TABLES]
SLOT_FEATURES = [0] + [t + 1 for t in GATHER_TABLES] + [t + 1 for t in ONEHOT_TABLES]
NG, NH = len(GATHER_TABLES), len(ONEHOT_TABLES)
NT = NG + 1
GROUP = 4
GROUPS = [range(g, min(g + GROUP, NT)) for g in range(0, NT, GROUP)]

QUAD = 32
QUADS = P // QUAD
HALF = QUAD // 2

LANES = SLOTS - 1
STEPS = (SLOTS + 1) // 2
PAIR_CHUNKS = 4
PAIR_LANE_GROUPS = -(-STEPS // PAIR_CHUNKS)


def pair_rows():
    chunks = []
    for c in range(PAIR_CHUNKS):
        rows = []
        for k in range(c + 1, STEPS + 1, PAIR_CHUNKS):
            lanes = LANES if k < STEPS else LANES // 2
            rows += [divmod((SLOTS + 1) * i + k, SLOTS) for i in range(lanes)]
        chunks.append(rows)
    flat = [frozenset(r) for rows in chunks for r in rows]
    assert len(flat) == len(set(flat)) == SLOTS * (SLOTS - 1) // 2
    return chunks


PAIR_ROWS = pair_rows()


def steps():
    order, onehots = [], list(range(NH))
    for t in range(2):
        for g in range(len(GROUPS)):
            if onehots:
                order.append(("onehot", onehots.pop(0)))
            order.append(("transpose", t, g))
    order += [("onehot", i) for i in onehots]
    order += [("gram", 0), ("gram", 1)]
    for t in range(2, TILES):
        order += [("transpose", t, g) for g in range(len(GROUPS) - 1)]
        order += [("layer1", t - 2), ("layer2", t - 2), ("layer3", t - 2)]
        order += [("transpose", t, len(GROUPS) - 1), ("gram", t)]
    for t in range(TILES - 2, TILES):
        order += [("layer1", t), ("layer2", t), ("layer3", t)]
    return order


def dlrm_tower(nc, dense, ids, onehot_ids, tables, w_pairs, w_dense, b1, w2, b2, w3, out):
    order = steps()
    units = [s for s in order if s[0] in ("onehot", "transpose")]
    unit_of = {s: u for u, s in enumerate(units)}
    last_unit = [max(unit_of[s] for s in units if s[0] == "onehot" or s[1] <= t) for t in range(TILES)]
    BANKS = 3

    scratch = nc.dram_tensor("pair_scratch", [TILES, SLOTS * SLOTS, P], F32, kind="Internal").ap()

    with ExitStack() as ctx:
        def sb(name, shape, dt=F32):
            return ctx.enter_context(nc.sbuf_tensor(name, shape, dt))

        def sem(name):
            return ctx.enter_context(nc.semaphore(name))

        emb = sb("emb", [P, BATCH, SLOTS])
        dense_rows = sb("dense_rows", [P, TILES, D])
        rows = sb("rows", [P, 2, NG, D])
        gather_ids = sb("gather_ids", [P, TILES, TABLES], I32)
        match_ids = sb("match_ids", [ONEHOT_PARTS, NH, BATCH], I32)
        RAW = 3
        table_raw = sb("table_raw", [ONEHOT_PARTS, RAW, ONEHOT_CHUNKS * D])
        table_hi = sb("table_hi", [ONEHOT_PARTS, 2, ONEHOT_CHUNKS * D], F32R)
        table_lo = sb("table_lo", [ONEHOT_PARTS, 2, ONEHOT_CHUNKS * D], F32R)
        onehot = sb("onehot", [ONEHOT_PARTS, 2, ONEHOT_CHUNKS, BATCH], F32R)
        row_no_int = sb("row_no_int", [ONEHOT_PARTS, ONEHOT_CHUNKS], I32)
        row_no = sb("row_no", [ONEHOT_PARTS, ONEHOT_CHUNKS])
        identity = sb("identity", [P, P])
        gram_rows = sb("gram_rows", [SLOTS, SLOTS, P])
        pairs = sb("pairs", [P, 2, PAIR_CHUNKS, P])
        w1_pairs = sb("w1_pairs", [P, PAIR_CHUNKS, N1])
        w1_dense_parts = sb("w1_dense_parts", [P, 2, N1])
        w1_dense = sb("w1_dense", [P, N1])
        w2_sb = sb("w2_sb", [P, N1_BLOCKS, N2])
        w3_sb = sb("w3_sb", [P, N2_BLOCKS])
        b1_sb = sb("b1_sb", [P, N1_BLOCKS])
        b2_sb = sb("b2_sb", [P, N2_BLOCKS])
        hidden1 = sb("hidden1", [P, N1_BLOCKS, P])
        hidden2 = sb("hidden2", [P, N2_BLOCKS, P])
        y_row = sb("y_row", [1, BATCH])

        def psum(name):
            return ctx.enter_context(nc.psum_tensor(name, [P, 512], F32))

        unit_bank = [psum(f"unit_bank{i}") for i in range(BANKS)]
        gram_bank = [psum(f"gram_bank{i}") for i in range(2)]
        layer1_bank = [psum(f"layer1_bank{i}") for i in range(2)]
        layer23_bank = psum("layer23_bank")

        def layer1_psum(n):
            return layer1_bank[n // 2][:, (n % 2) * P:(n % 2 + 1) * P]

        y_psum = layer23_bank[0:1, N2:N2 + P]

        ids_loaded = sem("ids_loaded")
        dense_loaded = sem("dense_loaded")
        onehot_in_loaded = [sem(f"onehot_in_loaded{i}") for i in range(NH)]
        weights1_loaded = sem("weights1_loaded")
        weights23_loaded = sem("weights23_loaded")
        identity_zeroed = sem("identity_zeroed")
        identity_ready = sem("identity_ready")
        row_no_made = sem("row_no_made")
        row_no_ready = sem("row_no_ready")
        gathered = {(t, g): sem(f"gathered{t}_{g}") for t in range(TILES) for g in range(len(GROUPS))}
        hi_ready = sem("hi_ready")
        lo_ready = sem("lo_ready")
        onehot_ready = sem("onehot_ready")
        w1_dense_ready = sem("w1_dense_ready")
        unit_filled = sem("unit_filled")
        unit_copied = sem("unit_copied")
        gram_filled = sem("gram_filled")
        gram_copied_act = sem("gram_copied_act")
        gram_copied_dve = sem("gram_copied_dve")
        pairs_stored = sem("pairs_stored")
        pairs_loaded = [sem(f"pairs_loaded{t}") for t in range(TILES)]
        layer1_filled = sem("layer1_filled")
        hidden1_act = sem("hidden1_act")
        hidden1_dve = sem("hidden1_dve")
        layer2_filled = sem("layer2_filled")
        hidden2_ready = sem("hidden2_ready")
        y_filled = sem("y_filled")
        y_copied = sem("y_copied")
        out_stored = sem("out_stored")

        block = ctx.enter_context(nc.Block())

        def load_onehot_inputs(eng, i):
            if i >= RAW:
                eng.wait_ge(lo_ready, i - RAW + 1)
            eng.dma_start(table_raw[:, i % RAW, :],
                          tables[ONEHOT_TABLES[i]].rearrange("(p c) d -> p (c d)", c=ONEHOT_CHUNKS)) \
               .then_inc(onehot_in_loaded[i], 16)
            eng.dma_start(match_ids[:, i, :],
                          onehot_ids[i:i + 1, :].to_broadcast([ONEHOT_PARTS, BATCH])) \
               .then_inc(onehot_in_loaded[i], 16)

        @block.sync
        def _(sp):
            sp.dma_start(gather_ids[:, :, :], ids.rearrange("(t p) f -> p t f", p=P)).then_inc(ids_loaded, 16)
            load_onehot_inputs(sp, 0)
            sp.dma_start(dense_rows[:, :, :], dense.rearrange("(t p) d -> p t d", p=P)).then_inc(dense_loaded, 16)
            for i in range(1, RAW):
                load_onehot_inputs(sp, i)
            sp.dma_start(w1_dense_parts[:, :, :], w_dense.rearrange("(a p) n -> p a n", p=P)) \
              .then_inc(weights1_loaded, 16)
            at = 0
            for c, chunk in enumerate(PAIR_ROWS):
                sp.dma_start(w1_pairs[0:len(chunk), c, :], w_pairs[at:at + len(chunk), :]) \
                  .then_inc(weights1_loaded, 16)
                at += len(chunk)
            sp.dma_start(b1_sb[:, :], b1).then_inc(weights1_loaded, 16)
            sp.dma_start(w2_sb[:, :, :], w2.rearrange("(a p) n -> p a n", p=P)).then_inc(weights23_loaded, 16)
            sp.dma_start(b2_sb[:, :], b2).then_inc(weights23_loaded, 16)
            sp.dma_start(w3_sb[:, :], w3).then_inc(weights23_loaded, 16)
            for i in range(RAW, NH):
                load_onehot_inputs(sp, i)
            for t in range(TILES):
                sp.wait_ge(gram_copied_act, t + 1)
                sp.wait_ge(gram_copied_dve, t + 1)
                sp.dma_start(scratch[t].rearrange("(a b) s -> a (b s)", a=SLOTS),
                             gram_rows[:, :, :].rearrange("a b s -> a (b s)")).then_inc(pairs_stored, 16)
                sp.wait_ge(pairs_stored, 16 * (t + 1))
                if t >= 2:
                    sp.wait_ge(layer1_filled, t - 1)
                for j in range(PAIR_LANE_GROUPS):
                    first = PAIR_CHUNKS * j + 1
                    count = min(PAIR_CHUNKS, STEPS + 1 - first)
                    source = bass.AP(scratch.tensor, (t * SLOTS * SLOTS + first) * P,
                                     [[(SLOTS + 1) * P, LANES], [1, count * P]])
                    sp.dma_start(pairs[LANES * j:LANES * (j + 1), t % 2, 0:count, :]
                                 .rearrange("i c s -> i (c s)"), source).then_inc(pairs_loaded[t], 16)
            sp.wait_ge(y_copied, TILES)
            sp.dma_start(out.rearrange("s one -> one s"), y_row[:, :]).then_inc(out_stored, 16)
            sp.wait_ge(out_stored, 16)

        @block.gpsimd
        def _(pool):
            nc.gpsimd.iota(row_no_int[:, :], pattern=[[1, ONEHOT_CHUNKS]], base=0,
                           channel_multiplier=ONEHOT_CHUNKS).then_inc(row_no_made, 1)
            nc.gpsimd.memset(identity[:, :], 0.0).then_inc(identity_zeroed, 1)
            pool.wait_ge(identity_zeroed, 1)
            nc.gpsimd.affine_select(out=identity[:, :], in_=identity[:, :], compare_op=ALU.not_equal,
                                    fill=1.0, base=0, pattern=[[-1, P]], channel_multiplier=1) \
                     .then_inc(identity_ready, 1)
            pool.wait_ge(ids_loaded, 16)
            for t in range(TILES):
                for g, group in enumerate(GROUPS):
                    if t >= 2:
                        pool.wait_ge(unit_filled, unit_of[("transpose", t - 2, g)] + 1)
                    for slot in group:
                        if slot == 0:
                            continue
                        table = GATHER_TABLES[slot - 1]
                        pool.indirect_dma_start(
                            rows[:, t % 2, slot - 1, :], None, tables[table],
                            bass.IndirectOffsetOnAxis(ap=gather_ids[:, t, table:table + 1], axis=0),
                        ).then_inc(gathered[(t, g)], 16)

        @block.tensor
        def _(pe):
            def fill_onehot(i):
                u = unit_of[("onehot", i)]
                bank = unit_bank[u % BANKS]
                if u >= BANKS:
                    pe.wait_ge(unit_copied, u - BANKS + 1)
                pe.wait_ge(hi_ready, i + 1)
                pe.wait_ge(lo_ready, i + 1)
                for c in range(ONEHOT_CHUNKS):
                    pe.wait_ge(onehot_ready, i * ONEHOT_CHUNKS + c + 1)
                    for part in (table_lo, table_hi):
                        last = nc.tensor.matmul(bank[:, :], part[:, i % 2, c * D:(c + 1) * D],
                                                onehot[:, i % 2, c, :],
                                                start=(c == 0 and part is table_lo),
                                                stop=(c == ONEHOT_CHUNKS - 1 and part is table_hi))
                last.then_inc(unit_filled, 1)

            def fill_transpose(t, g):
                u = unit_of[("transpose", t, g)]
                bank = unit_bank[u % BANKS]
                if u == 0 or units[:u] == [s for s in units[:u] if s[0] == "onehot"]:
                    pe.wait_ge(identity_ready, 1)
                if u >= BANKS:
                    pe.wait_ge(unit_copied, u - BANKS + 1)
                if g == 0:
                    pe.wait_ge(dense_loaded, 16)
                pe.wait_ge(gathered[(t, g)], 16 * sum(slot > 0 for slot in GROUPS[g]))
                for n, slot in enumerate(GROUPS[g]):
                    source = rows[:, t % 2, slot - 1, :] if slot else dense_rows[:, t, :]
                    last = nc.tensor.transpose(bank[:, n * P:(n + 1) * P], source, identity[:, :])
                last.then_inc(unit_filled, 1)

            def fill_gram(t):
                pe.wait_ge(unit_copied, last_unit[t] + 1)
                if t >= 1:
                    pe.wait_ge(gram_copied_act, t)
                    pe.wait_ge(gram_copied_dve, t)
                for q in range(QUAD):
                    for s in range(QUADS):
                        vectors = emb[:, t * P + QUAD * s + q, :]
                        last = nc.tensor.matmul(
                            gram_bank[q // HALF][QUAD * s:QUAD * s + SLOTS,
                                                 (q % HALF) * SLOTS:(q % HALF + 1) * SLOTS],
                            vectors, vectors, start=True, stop=True)
                    if q % HALF == HALF - 1:
                        last.then_inc(gram_filled, 1)

            def fill_layer1(t):
                if t == 0:
                    pe.wait_ge(weights1_loaded, 16 * (2 + PAIR_CHUNKS))
                    pe.wait_ge(w1_dense_ready, 1)
                if t >= 1:
                    pe.wait_ge(hidden1_act, t)
                    pe.wait_ge(hidden1_dve, t)
                for n in range(N1_BLOCKS):
                    nc.tensor.matmul(layer1_psum(n), w1_dense[:, n * P:(n + 1) * P],
                                     emb[:, t * P:(t + 1) * P, 0], start=(n % 2 == 0), stop=False,
                                     skip_group_check=True)
                pe.wait_ge(pairs_loaded[t], 16 * PAIR_LANE_GROUPS)
                for n in range(N1_BLOCKS):
                    for c, chunk in enumerate(PAIR_ROWS):
                        last = nc.tensor.matmul(layer1_psum(n),
                                                w1_pairs[0:len(chunk), c, n * P:(n + 1) * P],
                                                pairs[0:len(chunk), t % 2, c, :],
                                                start=False, stop=(c == PAIR_CHUNKS - 1),
                                                skip_group_check=True)
                last.then_inc(layer1_filled, 1)

            def fill_layer2(t):
                if t == 0:
                    pe.wait_ge(weights23_loaded, 48)
                if t >= 1:
                    pe.wait_ge(y_copied, t)
                pe.wait_ge(hidden1_act, t + 1)
                pe.wait_ge(hidden1_dve, t + 1)
                for m in range(N2_BLOCKS):
                    for n in range(N1_BLOCKS):
                        last = nc.tensor.matmul(layer23_bank[:, m * P:(m + 1) * P],
                                                w2_sb[:, n, m * P:(m + 1) * P], hidden1[:, n, :],
                                                start=(n == 0), stop=(n == N1_BLOCKS - 1))
                last.then_inc(layer2_filled, 1)

            def fill_layer3(t):
                pe.wait_ge(hidden2_ready, t + 1)
                for m in range(N2_BLOCKS):
                    last = nc.tensor.matmul(y_psum, w3_sb[:, m:m + 1], hidden2[:, m, :],
                                            start=(m == 0), stop=(m == N2_BLOCKS - 1))
                last.then_inc(y_filled, 1)

            for step in order:
                if step[0] == "onehot":
                    fill_onehot(step[1])
                elif step[0] == "transpose":
                    fill_transpose(step[1], step[2])
                elif step[0] == "gram":
                    fill_gram(step[1])
                elif step[0] == "layer1":
                    fill_layer1(step[1])
                elif step[0] == "layer2":
                    fill_layer2(step[1])
                else:
                    fill_layer3(step[1])

        def gram_to_rows(copy, h, s):
            first = QUAD * s + HALF * h
            return copy(gram_rows[:, :, first:first + HALF],
                        gram_bank[h][QUAD * s:QUAD * s + SLOTS, 0:HALF * SLOTS]
                        .rearrange("a (q b) -> a b q", b=SLOTS))

        @block.scalar
        def _(act):
            def high_part(i):
                act.wait_ge(onehot_in_loaded[i], 32)
                if i >= 2:
                    act.wait_ge(unit_filled, unit_of[("onehot", i - 2)] + 1)
                nc.scalar.copy(table_hi[:, i % 2, :], table_raw[:, i % RAW, :]).then_inc(hi_ready, 1)

            high_part(0)
            high_part(1)
            for step in order:
                if step[0] in ("onehot", "transpose"):
                    u = unit_of[step]
                    act.wait_ge(unit_filled, u + 1)
                    if step[0] == "onehot":
                        slot = NT + step[1]
                        nc.scalar.copy(emb[:, :, slot], unit_bank[u % BANKS][:, :]).then_inc(unit_copied, 1)
                        if step[1] + 2 < NH:
                            high_part(step[1] + 2)
                    else:
                        _, t, g = step
                        slots = GROUPS[g]
                        nc.scalar.copy(
                            emb[:, t * P:(t + 1) * P, slots[0]:slots[-1] + 1].rearrange("d s n -> d n s"),
                            unit_bank[u % BANKS][:, 0:len(slots) * P].rearrange("d (n s) -> d n s", s=P),
                        ).then_inc(unit_copied, 1)
                elif step[0] == "gram":
                    t = step[1]
                    if t >= 1:
                        act.wait_ge(pairs_stored, 16 * t)
                    for h in range(2):
                        act.wait_ge(gram_filled, 2 * t + h + 1)
                        for s in (2, 3):
                            last = gram_to_rows(nc.scalar.copy, h, s)
                    last.then_inc(gram_copied_act, 1)
                elif step[0] == "layer1":
                    t = step[1]
                    act.wait_ge(layer1_filled, t + 1)
                    if t >= 1:
                        act.wait_ge(layer2_filled, t)
                    if t == 0:
                        act.wait_ge(weights1_loaded, 16 * (2 + PAIR_CHUNKS))
                    for n in (0, 1):
                        last = nc.scalar.activation(hidden1[:, n, :], layer1_psum(n),
                                                    ACT.Relu, bias=b1_sb[:, n:n + 1])
                    last.then_inc(hidden1_act, 1)

        @block.vector
        def _(dve):
            dve.wait_ge(row_no_made, 1)
            nc.vector.tensor_copy(row_no[:, :], row_no_int[:, :]).then_inc(row_no_ready, 1)
            dve.wait_ge(row_no_ready, 1)
            for i in range(NH):
                dve.wait_ge(onehot_in_loaded[i], 32)
                if i >= 2:
                    dve.wait_ge(unit_filled, unit_of[("onehot", i - 2)] + 1)
                dve.wait_ge(hi_ready, i + 1)
                nc.vector.tensor_tensor(table_lo[:, i % 2, :], table_raw[:, i % RAW, :],
                                        table_hi[:, i % 2, :].bitcast(F32), ALU.subtract) \
                         .then_inc(lo_ready, 1)
                for c in range(ONEHOT_CHUNKS):
                    nc.vector.tensor_scalar(onehot[:, i % 2, c, :], match_ids[:, i, :],
                                            row_no[:, c:c + 1], None, ALU.is_equal) \
                             .then_inc(onehot_ready, 1)
            dve.wait_ge(weights1_loaded, 16 * (2 + PAIR_CHUNKS))
            nc.vector.tensor_tensor(w1_dense[:, :], w1_dense_parts[:, 0, :], w1_dense_parts[:, 1, :],
                                    ALU.add).then_inc(w1_dense_ready, 1)
            for step in order:
                if step[0] == "gram":
                    t = step[1]
                    if t >= 1:
                        dve.wait_ge(pairs_stored, 16 * t)
                    for h in range(2):
                        dve.wait_ge(gram_filled, 2 * t + h + 1)
                        for s in (0, 1):
                            last = gram_to_rows(nc.vector.tensor_copy, h, s)
                    last.then_inc(gram_copied_dve, 1)
                elif step[0] == "layer1":
                    t = step[1]
                    dve.wait_ge(layer1_filled, t + 1)
                    if t >= 1:
                        dve.wait_ge(layer2_filled, t)
                    for n in (2, 3):
                        last = nc.vector.tensor_scalar(hidden1[:, n, :], layer1_psum(n),
                                                       b1_sb[:, n:n + 1], 0.0, ALU.add, ALU.max)
                    last.then_inc(hidden1_dve, 1)
                elif step[0] == "layer2":
                    t = step[1]
                    if t == 0:
                        dve.wait_ge(weights23_loaded, 48)
                    dve.wait_ge(layer2_filled, t + 1)
                    if t >= 1:
                        dve.wait_ge(y_filled, t)
                    for m in range(N2_BLOCKS):
                        last = nc.vector.tensor_scalar(hidden2[:, m, :], layer23_bank[:, m * P:(m + 1) * P],
                                                       b2_sb[:, m:m + 1], 0.0, ALU.add, ALU.max)
                    last.then_inc(hidden2_ready, 1)
                elif step[0] == "layer3":
                    t = step[1]
                    dve.wait_ge(y_filled, t + 1)
                    nc.vector.tensor_copy(y_row[:, t * P:(t + 1) * P], y_psum).then_inc(y_copied, 1)


def kernel(**inputs):
    import concourse.bacc as bacc
    from concourse.bass_utils import run_bass_kernel_spmd

    pair_of = {p: n for n, p in enumerate(zip(*np.triu_indices(SLOTS, k=1)))}
    w1 = np.asarray(inputs["W_top1"])
    w_rows = [D + pair_of[tuple(sorted((SLOT_FEATURES[a], SLOT_FEATURES[b])))]
              for chunk in PAIR_ROWS for a, b in chunk]
    ids = np.asarray(inputs["ids"])
    arrays = {
        "dense": np.asarray(inputs["r_dense_features"]),
        "ids": ids,
        "onehot_ids": np.ascontiguousarray(ids.T[ONEHOT_TABLES]),
        "w_pairs": w1[w_rows],
        "w_dense": np.concatenate([w1[:D], w1[-D:]]),
        "b1": np.ascontiguousarray(np.asarray(inputs["b_top1"]).reshape(N1_BLOCKS, P).T),
        "w2": np.asarray(inputs["W_top2"]),
        "b2": np.ascontiguousarray(np.asarray(inputs["b_top2"]).reshape(N2_BLOCKS, P).T),
        "w3": np.ascontiguousarray(np.asarray(inputs["W_top3"]).reshape(N2_BLOCKS, P).T),
    }
    tables = {f"tbl_{n}": np.asarray(inputs[f"tbl_{n}"]) for n in range(TABLES)}

    nc = bacc.Bacc("TRN2", target_bir_lowering=False, num_devices=1)

    def dram(name, a):
        return nc.dram_tensor(name, a.shape, mybir.dt.from_np(a.dtype), kind="ExternalInput").ap()

    given = {name: dram(name, a) for name, a in arrays.items()}
    given["tables"] = [dram(name, a) for name, a in tables.items()]
    given["out"] = nc.dram_tensor("y", (BATCH, 1), F32, kind="ExternalOutput").ap()
    dlrm_tower(nc, **given)
    result = run_bass_kernel_spmd(nc, [{**arrays, **tables}], core_ids=[0])
    return result.results[0]["y"]
```

```python
from contextlib import ExitStack

import numpy as np

import concourse.bass as bass
from concourse import mybir

F32 = mybir.dt.float32
F32R = mybir.dt.float32r
I32 = mybir.dt.int32
ALU = mybir.AluOpType
ACT = mybir.ActivationFunctionType

P = 128
BATCH = 512
TABLES = 26
SLOTS = TABLES + 1
D = 128
TILES = BATCH // P
N1, N2 = 512, 256
N1_BLOCKS, N2_BLOCKS = N1 // P, N2 // P

ONEHOT_TABLES = [13, 16, 17, 19, 20, 21, 22, 23, 24]
ONEHOT_ROWS = 1000
ONEHOT_CHUNKS = 8
ONEHOT_PARTS = ONEHOT_ROWS // ONEHOT_CHUNKS
GATHER_TABLES = [t for t in range(TABLES) if t not in ONEHOT_TABLES]
SLOT_FEATURES = [0] + [t + 1 for t in GATHER_TABLES] + [t + 1 for t in ONEHOT_TABLES]
NG, NH = len(GATHER_TABLES), len(ONEHOT_TABLES)
NT = NG + 1
GROUP = 4
GROUPS = [range(g, min(g + GROUP, NT)) for g in range(0, NT, GROUP)]

QUAD = 32
QUADS = P // QUAD
HALF = QUAD // 2

LANES = SLOTS - 1
HALF_LANES = LANES // 2
STEPS = (SLOTS + 1) // 2
CHUNKS = 3
PAIR_READS = [(LANES * j, LANES, 0, CHUNKS, 0, CHUNKS * j + 1) for j in range(4)]
PAIR_READS += [(4 * LANES, HALF_LANES, 0, 2, 0, STEPS - 1),
               (4 * LANES, HALF_LANES, 2, 1, HALF_LANES, STEPS - 1)]
SP_READS = 4
PAIR_PARTS = 4 * LANES + HALF_LANES


def pair_rows():
    place = {}
    for part, lanes, chunk, chunks, i, k in PAIR_READS:
        for lane in range(lanes):
            for c in range(chunks):
                place[(chunk + c, part + lane)] = divmod((SLOTS + 1) * (i + lane) + k + c, SLOTS)
    rows = [place[(c, p)] for c in range(CHUNKS) for p in range(PAIR_PARTS)]
    assert len({frozenset(r) for r in rows}) == len(rows) == SLOTS * (SLOTS - 1) // 2
    return rows


PAIR_ROWS = pair_rows()


def steps():
    def transposes(t, first=0, last=len(GROUPS)):
        return [("transpose", t, g) for g in range(first, last)]

    def gram(t):
        return [("gram", t, 0), ("gram", t, 1)]

    early = transposes(0) + transposes(1)
    order = [("onehot", 0)]
    for i in range(1, NH):
        order += [("onehot", i)] + early[:1]
        early = early[1:]
    order += [("gram", 0, 0)] + early[:1] + [("gram", 0, 1)] + early[1:] + gram(1)
    order += transposes(2)
    order += [("layer1_dense", 0), ("layer1", 0, 0), ("gram", 2, 0), ("layer1", 0, 1), ("gram", 2, 1)]
    order += [("layer2", 0)] + transposes(3, 0, 1)
    order += [("layer1_dense", 1), ("layer1", 1, 0), ("layer3", 0), ("layer1", 1, 1)]
    order += [("transpose", 3, 1), ("transpose", 3, 2), ("layer2", 1), ("transpose", 3, 3), ("layer3", 1)]
    order += transposes(3, 4) + gram(3)
    for t in (2, 3):
        order += [("layer1_dense", t), ("layer1", t, 0), ("layer1", t, 1), ("layer2", t), ("layer3", t)]
    return order


def dlrm_tower(nc, dense, ids, onehot_ids, tables, w_pairs, w_dense, b1, w2, b2, w3, out):
    order = steps()
    units = [s for s in order if s[0] in ("onehot", "transpose")]
    unit_of = {s: u for u, s in enumerate(units)}
    units_before = [sum(s in unit_of for s in order[:order.index(("gram", t, 0))]) for t in range(TILES)]
    for t, n in enumerate(units_before):
        assert all(unit_of[s] < n for s in units if s[0] == "onehot" or s[1] <= t)
    bank_no, turns = {}, [0, 0]
    for s in units:
        borrows = int(s[0] == "transpose" and unit_of[s] < units_before[0])
        bank_no[s] = 2 * borrows + turns[borrows] % 2
        turns[borrows] += 1

    def units_before_reuse(step):
        earlier = [u for u in range(unit_of[step]) if bank_no[units[u]] == bank_no[step]]
        return earlier[-1] + 1 if earlier else 0

    scratch = nc.dram_tensor("pair_scratch", [TILES, SLOTS * SLOTS, P], F32, kind="Internal").ap()

    with ExitStack() as ctx:
        def sb(name, shape, dt=F32):
            return ctx.enter_context(nc.sbuf_tensor(name, shape, dt))

        def sem(name):
            return ctx.enter_context(nc.semaphore(name))

        emb = sb("emb", [P, BATCH, SLOTS])
        dense_rows = sb("dense_rows", [P, TILES, D])
        rows = sb("rows", [P, 2, NG, D])
        gather_ids = sb("gather_ids", [P, TILES, TABLES], I32)
        match_ids = sb("match_ids", [ONEHOT_PARTS, NH, BATCH], I32)
        RAW = 3
        table_raw = sb("table_raw", [ONEHOT_PARTS, RAW, ONEHOT_CHUNKS * D])
        table_hi = sb("table_hi", [ONEHOT_PARTS, 2, ONEHOT_CHUNKS * D], F32R)
        table_lo = sb("table_lo", [ONEHOT_PARTS, 2, ONEHOT_CHUNKS * D], F32R)
        onehot = sb("onehot", [ONEHOT_PARTS, 2, ONEHOT_CHUNKS, BATCH], F32R)
        shifted_ids = sb("shifted_ids", [ONEHOT_PARTS, 2, BATCH])
        first_row_int = sb("first_row_int", [ONEHOT_PARTS, 1], I32)
        warm_up = sb("warm_up", [ONEHOT_PARTS, 1])
        minus_first_row = sb("minus_first_row", [ONEHOT_PARTS, 1])
        identity = sb("identity", [P, P])
        gram_rows = sb("gram_rows", [SLOTS, SLOTS, P])
        pairs = sb("pairs", [PAIR_PARTS, 2, CHUNKS, P])
        w1_pairs = sb("w1_pairs", [PAIR_PARTS, CHUNKS, N1])
        w1_dense_parts = sb("w1_dense_parts", [P, 2, N1])
        w1_dense = sb("w1_dense", [P, N1])
        w2_sb = sb("w2_sb", [P, N1_BLOCKS, N2])
        w3_sb = sb("w3_sb", [P, N2_BLOCKS])
        b1_sb = sb("b1_sb", [P, N1_BLOCKS])
        b2_sb = sb("b2_sb", [P, N2_BLOCKS])
        hidden1 = sb("hidden1", [P, N1_BLOCKS, P])
        hidden2 = sb("hidden2", [P, N2_BLOCKS, P])
        y_row = sb("y_row", [1, BATCH])

        def psum(name):
            return ctx.enter_context(nc.psum_tensor(name, [P, 512], F32))

        unit_bank = [psum(f"unit_bank{i}") for i in range(2)]
        gram_bank = [psum(f"gram_bank{i}") for i in range(2)]
        layer1_bank = [psum(f"layer1_bank{i}") for i in range(2)]
        layer2_bank = [psum(f"layer2_bank{i}") for i in range(N2_BLOCKS)]

        def layer1_psum(n):
            return layer1_bank[n // 2][:, (n % 2) * P:(n % 2 + 1) * P]

        def bank_of(step):
            return (unit_bank + gram_bank)[bank_no[step]]

        y_psum = layer2_bank[0][0:1, P:2 * P]

        ids_loaded = sem("ids_loaded")
        dense_loaded = sem("dense_loaded")
        match_ids_loaded = [sem(f"match_ids_loaded{i}") for i in range(NH)]
        table_loaded = [sem(f"table_loaded{i}") for i in range(NH)]
        second_half_loaded = sem("second_half_loaded")
        weights1_loaded = sem("weights1_loaded")
        weights23_loaded = sem("weights23_loaded")
        identity_zeroed = sem("identity_zeroed")
        identity_ready = sem("identity_ready")
        first_row_made = sem("first_row_made")
        first_row_ready = sem("first_row_ready")
        shifted_ready = sem("shifted_ready")
        gathered = {(t, g): sem(f"gathered{t}_{g}") for t in range(TILES) for g in range(len(GROUPS))}
        hi_ready = sem("hi_ready")
        lo_ready = sem("lo_ready")
        onehot_ready = sem("onehot_ready")
        w1_dense_ready = sem("w1_dense_ready")
        unit_filled = sem("unit_filled")
        unit_copied = sem("unit_copied")
        gram_filled = sem("gram_filled")
        gram_copied_act = sem("gram_copied_act")
        gram_copied_dve = sem("gram_copied_dve")
        pairs_stored = sem("pairs_stored")
        pairs_loaded = [sem(f"pairs_loaded{t}") for t in range(TILES)]
        pairs_loaded_pool = sem("pairs_loaded_pool")
        layer1_filled = sem("layer1_filled")
        hidden1_act = sem("hidden1_act")
        hidden1_dve = sem("hidden1_dve")
        layer2_filled = sem("layer2_filled")
        hidden2_act = sem("hidden2_act")
        hidden2_dve = sem("hidden2_dve")
        y_filled = sem("y_filled")
        y_copied = sem("y_copied")
        out_stored = sem("out_stored")

        block = ctx.enter_context(nc.Block())

        def table_pieces(i):
            width = ONEHOT_CHUNKS * D
            return [slice(0, width // 2), slice(width // 2, width)] if i == 0 else [slice(0, width)]

        def load_onehot_inputs(eng, i):
            if i >= RAW:
                eng.wait_ge(lo_ready, i - RAW + 1)
            eng.dma_start(match_ids[:, i, :],
                          onehot_ids[i:i + 1, :].to_broadcast([ONEHOT_PARTS, BATCH])) \
               .then_inc(match_ids_loaded[i], 16)
            source = tables[ONEHOT_TABLES[i]].rearrange("(p c) d -> p (c d)", c=ONEHOT_CHUNKS)
            for half, loaded in zip(table_pieces(i), (table_loaded[i], second_half_loaded)):
                eng.dma_start(table_raw[:, i % RAW, half], source[:, half]).then_inc(loaded, 16)

        def load_pairs(eng, t, read):
            part, lanes, chunk, chunks, i, k = read
            source = bass.AP(scratch.tensor, (t * SLOTS * SLOTS + (SLOTS + 1) * i + k) * P,
                             [[(SLOTS + 1) * P, lanes], [1, chunks * P]])
            return eng.dma_start(pairs[part:part + lanes, t % 2, chunk:chunk + chunks, :]
                                 .rearrange("i c s -> i (c s)"), source)

        @block.sync
        def _(sp):
            sp.dma_start(gather_ids[:, :, :], ids.rearrange("(t p) f -> p t f", p=P)).then_inc(ids_loaded, 16)
            load_onehot_inputs(sp, 0)
            load_onehot_inputs(sp, 1)
            sp.dma_start(dense_rows[:, :, :], dense.rearrange("(t p) d -> p t d", p=P)).then_inc(dense_loaded, 16)
            for i in range(2, RAW):
                load_onehot_inputs(sp, i)
            for i in range(RAW, NH):
                load_onehot_inputs(sp, i)
            sp.dma_start(w1_dense_parts[:, :, :], w_dense.rearrange("(a p) n -> p a n", p=P)) \
              .then_inc(weights1_loaded, 16)
            sp.dma_start(w1_pairs[:, :, :], w_pairs.rearrange("(c p) n -> p c n", c=CHUNKS)) \
              .then_inc(weights1_loaded, 16)
            sp.dma_start(b1_sb[:, :], b1).then_inc(weights1_loaded, 16)
            sp.dma_start(w2_sb[:, :, :], w2.rearrange("(a p) n -> p a n", p=P)).then_inc(weights23_loaded, 16)
            sp.dma_start(b2_sb[:, :], b2).then_inc(weights23_loaded, 16)
            sp.dma_start(w3_sb[:, :], w3).then_inc(weights23_loaded, 16)
            for t in range(TILES):
                sp.wait_ge(gram_copied_act, 2 * t + 2)
                sp.wait_ge(gram_copied_dve, 2 * t + 2)
                sp.dma_start(scratch[t].rearrange("(a b) s -> a (b s)", a=SLOTS),
                             gram_rows[:, :, :].rearrange("a b s -> a (b s)")).then_inc(pairs_stored, 16)
                sp.wait_ge(pairs_stored, 16 * (t + 1))
                if t >= 2:
                    sp.wait_ge(layer1_filled, 2 * (t - 1))
                for read in PAIR_READS if t < TILES - 1 else PAIR_READS[:SP_READS]:
                    load_pairs(sp, t, read).then_inc(pairs_loaded[t], 16)
            sp.wait_ge(y_copied, TILES)
            sp.dma_start(out.rearrange("s one -> one s"), y_row[:, :]).then_inc(out_stored, 16)
            sp.wait_ge(out_stored, 16)

        @block.gpsimd
        def _(pool):
            nc.gpsimd.iota(first_row_int[:, :], pattern=[[1, 1]], base=0,
                           channel_multiplier=-ONEHOT_CHUNKS).then_inc(first_row_made, 1)
            nc.gpsimd.memset(identity[:, :], 0.0).then_inc(identity_zeroed, 1)
            pool.wait_ge(identity_zeroed, 1)
            nc.gpsimd.affine_select(out=identity[:, :], in_=identity[:, :], compare_op=ALU.not_equal,
                                    fill=1.0, base=0, pattern=[[-1, P]], channel_multiplier=1) \
                     .then_inc(identity_ready, 1)
            pool.wait_ge(ids_loaded, 16)
            for t in range(TILES):
                for g, group in enumerate(GROUPS):
                    if t >= 2:
                        pool.wait_ge(unit_filled, unit_of[("transpose", t - 2, g)] + 1)
                    for slot in group:
                        if slot == 0:
                            continue
                        table = GATHER_TABLES[slot - 1]
                        pool.indirect_dma_start(
                            rows[:, t % 2, slot - 1, :], None, tables[table],
                            bass.IndirectOffsetOnAxis(ap=gather_ids[:, t, table:table + 1], axis=0),
                        ).then_inc(gathered[(t, g)], 16)

            pool.wait_ge(pairs_stored, 16 * TILES)
            pool.wait_ge(layer1_filled, 2 * (TILES - 2))
            for read in PAIR_READS[SP_READS:]:
                load_pairs(pool, TILES - 1, read).then_inc(pairs_loaded_pool, 16)

        @block.tensor
        def _(pe):
            def fill_onehot(i):
                step = ("onehot", i)
                bank = bank_of(step)
                if units_before_reuse(step):
                    pe.wait_ge(unit_copied, units_before_reuse(step))
                for part in (table_hi, table_lo):
                    if part is table_lo:
                        pe.wait_ge(lo_ready, i + 1)
                    for c in range(ONEHOT_CHUNKS):
                        if part is table_hi:
                            if i or c == 0:
                                pe.wait_ge(hi_ready, i + 1 + (i > 0))
                            elif c == ONEHOT_CHUNKS // 2:
                                pe.wait_ge(hi_ready, 2)
                            pe.wait_ge(onehot_ready, i * ONEHOT_CHUNKS + c + 1)
                        last = nc.tensor.matmul(bank[:, :], part[:, i % 2, c * D:(c + 1) * D],
                                                onehot[:, i % 2, c, :],
                                                start=(c == 0 and part is table_hi),
                                                stop=(c == ONEHOT_CHUNKS - 1 and part is table_lo))
                last.then_inc(unit_filled, 1)

            def fill_transpose(t, g):
                step = ("transpose", t, g)
                bank = bank_of(step)
                if (t, g) == (0, 0):
                    pe.wait_ge(identity_ready, 1)
                if units_before_reuse(step):
                    pe.wait_ge(unit_copied, units_before_reuse(step))
                if g == 0:
                    pe.wait_ge(dense_loaded, 16)
                pe.wait_ge(gathered[(t, g)], 16 * sum(slot > 0 for slot in GROUPS[g]))
                for n, slot in enumerate(GROUPS[g]):
                    source = rows[:, t % 2, slot - 1, :] if slot else dense_rows[:, t, :]
                    last = nc.tensor.transpose(bank[:, n * P:(n + 1) * P], source, identity[:, :])
                last.then_inc(unit_filled, 1)

            def fill_gram(t, h):
                pe.wait_ge(unit_copied, units_before[t])
                if t >= 1:
                    pe.wait_ge(gram_copied_act, 2 * (t - 1) + h + 1)
                    pe.wait_ge(gram_copied_dve, 2 * (t - 1) + h + 1)
                for q in range(HALF * h, HALF * (h + 1)):
                    for s in range(QUADS):
                        vectors = emb[:, t * P + QUAD * s + q, :]
                        last = nc.tensor.matmul(
                            gram_bank[h][QUAD * s:QUAD * s + SLOTS,
                                                 (q % HALF) * SLOTS:(q % HALF + 1) * SLOTS],
                            vectors, vectors, start=True, stop=True)
                last.then_inc(gram_filled, 1)

            def fill_layer1_dense(t):
                if t == 0:
                    pe.wait_ge(w1_dense_ready, 1)
                for n in range(N1_BLOCKS):
                    if t >= 1 and n % 2 == 0:
                        pe.wait_ge((hidden1_act, hidden1_dve)[n // 2], t)
                    nc.tensor.matmul(layer1_psum(n), w1_dense[:, n * P:(n + 1) * P],
                                     emb[:, t * P:(t + 1) * P, 0], start=(n % 2 == 0), stop=False,
                                     skip_group_check=True)

            def fill_layer1(t, half):
                if t == 0:
                    pe.wait_ge(weights1_loaded, 48)
                pe.wait_ge(pairs_loaded[t], 16 * (len(PAIR_READS) if t < TILES - 1 else SP_READS))
                if t == TILES - 1:
                    pe.wait_ge(pairs_loaded_pool, 16 * (len(PAIR_READS) - SP_READS))
                for n in range(2 * half, 2 * half + 2):
                    for c in range(CHUNKS):
                        last = nc.tensor.matmul(layer1_psum(n), w1_pairs[:, c, n * P:(n + 1) * P],
                                                pairs[:, t % 2, c, :],
                                                start=False, stop=(c == CHUNKS - 1),
                                                skip_group_check=True)
                last.then_inc(layer1_filled, 1)

            def fill_layer2(t):
                if t == 0:
                    pe.wait_ge(weights23_loaded, 48)
                for m in range(N2_BLOCKS):
                    if t >= 1:
                        pe.wait_ge((hidden2_act, hidden2_dve)[m], t)
                        if m == 0:
                            pe.wait_ge(y_copied, t)
                    for n in range(N1_BLOCKS):
                        if m == 0 and n % 2 == 0:
                            pe.wait_ge((hidden1_act, hidden1_dve)[n // 2], t + 1)
                        last = nc.tensor.matmul(layer2_bank[m][:, 0:P],
                                                w2_sb[:, n, m * P:(m + 1) * P], hidden1[:, n, :],
                                                start=(n == 0), stop=(n == N1_BLOCKS - 1))
                    last.then_inc(layer2_filled, 1)

            def fill_layer3(t):
                for m in range(N2_BLOCKS):
                    pe.wait_ge((hidden2_act, hidden2_dve)[m], t + 1)
                    last = nc.tensor.matmul(y_psum, w3_sb[:, m:m + 1], hidden2[:, m, :],
                                            start=(m == 0), stop=(m == N2_BLOCKS - 1))
                last.then_inc(y_filled, 1)

            for step in order:
                if step[0] == "onehot":
                    fill_onehot(step[1])
                elif step[0] == "transpose":
                    fill_transpose(step[1], step[2])
                elif step[0] == "gram":
                    fill_gram(step[1], step[2])
                elif step[0] == "layer1_dense":
                    fill_layer1_dense(step[1])
                elif step[0] == "layer1":
                    fill_layer1(step[1], step[2])
                elif step[0] == "layer2":
                    fill_layer2(step[1])
                else:
                    fill_layer3(step[1])

        def gram_to_rows(copy, h, s):
            first = QUAD * s + HALF * h
            return copy(gram_rows[:, :, first:first + HALF],
                        gram_bank[h][QUAD * s:QUAD * s + SLOTS, 0:HALF * SLOTS]
                        .rearrange("a (q b) -> a b q", b=SLOTS))

        @block.scalar
        def _(act):
            def prepare_lookup(i):
                act.wait_ge(match_ids_loaded[i], 16)
                if i >= 2:
                    act.wait_ge(onehot_ready, ONEHOT_CHUNKS * (i - 1))
                nc.scalar.activation(shifted_ids[:, i % 2, :], match_ids[:, i, :], ACT.Identity,
                                     bias=minus_first_row[:, 0:1]).then_inc(shifted_ready, 1)
                if i >= 2:
                    act.wait_ge(unit_filled, unit_of[("onehot", i - 2)] + 1)
                for half, loaded in zip(table_pieces(i), (table_loaded[i], second_half_loaded)):
                    act.wait_ge(loaded, 16)
                    nc.scalar.copy(table_hi[:, i % 2, half], table_raw[:, i % RAW, half]).then_inc(hi_ready, 1)

            act.wait_ge(first_row_ready, 1)
            nc.scalar.activation(warm_up[:, :], minus_first_row[:, :], ACT.Identity)
            prepare_lookup(0)
            prepare_lookup(1)
            for step in order:
                if step[0] in ("onehot", "transpose"):
                    u = unit_of[step]
                    act.wait_ge(unit_filled, u + 1)
                    if step[0] == "onehot":
                        slot = NT + step[1]
                        nc.scalar.copy(emb[:, :, slot], bank_of(step)[:, :]).then_inc(unit_copied, 1)
                        if step[1] + 2 < NH:
                            prepare_lookup(step[1] + 2)
                    else:
                        _, t, g = step
                        slots = GROUPS[g]
                        nc.scalar.copy(
                            emb[:, t * P:(t + 1) * P, slots[0]:slots[-1] + 1].rearrange("d s n -> d n s"),
                            bank_of(step)[:, 0:len(slots) * P].rearrange("d (n s) -> d n s", s=P),
                        ).then_inc(unit_copied, 1)
                elif step[0] == "gram":
                    _, t, h = step
                    if t >= 1:
                        act.wait_ge(pairs_stored, 16 * t)
                    act.wait_ge(gram_filled, 2 * t + h + 1)
                    for s in (2, 3):
                        last = gram_to_rows(nc.scalar.copy, h, s)
                    last.then_inc(gram_copied_act, 1)
                elif step[0] == "layer1" and step[2] == 0:
                    t = step[1]
                    act.wait_ge(layer1_filled, 2 * t + 1)
                    if t >= 1:
                        act.wait_ge(layer2_filled, 2 * t)
                    if t == 0:
                        act.wait_ge(weights1_loaded, 48)
                    for n in (0, 1):
                        last = nc.scalar.activation(hidden1[:, n, :], layer1_psum(n),
                                                    ACT.Relu, bias=b1_sb[:, n:n + 1])
                    last.then_inc(hidden1_act, 1)
                elif step[0] == "layer2":
                    t = step[1]
                    if t == 0:
                        act.wait_ge(weights23_loaded, 48)
                    act.wait_ge(layer2_filled, 2 * t + 1)
                    if t >= 1:
                        act.wait_ge(y_filled, t)
                    nc.scalar.activation(hidden2[:, 0, :], layer2_bank[0][:, 0:P], ACT.Relu,
                                         bias=b2_sb[:, 0:1]).then_inc(hidden2_act, 1)

        @block.vector
        def _(dve):
            dve.wait_ge(first_row_made, 1)
            nc.vector.tensor_copy(minus_first_row[:, :], first_row_int[:, :]).then_inc(first_row_ready, 1)
            for i in range(NH):
                dve.wait_ge(shifted_ready, i + 1)
                if i >= 2:
                    dve.wait_ge(unit_filled, unit_of[("onehot", i - 2)] + 1)
                for c in range(ONEHOT_CHUNKS):
                    nc.vector.tensor_scalar(onehot[:, i % 2, c, :], shifted_ids[:, i % 2, :],
                                            float(c), None, ALU.is_equal) \
                             .then_inc(onehot_ready, 1)
                dve.wait_ge(table_loaded[i], 16)
                if i == 0:
                    dve.wait_ge(second_half_loaded, 16)
                dve.wait_ge(hi_ready, i + 2)
                nc.vector.tensor_tensor(table_lo[:, i % 2, :], table_raw[:, i % RAW, :],
                                        table_hi[:, i % 2, :].bitcast(F32), ALU.subtract) \
                         .then_inc(lo_ready, 1)
            for step in order:
                if step[0] == "gram":
                    _, t, h = step
                    if t >= 1:
                        dve.wait_ge(pairs_stored, 16 * t)
                    dve.wait_ge(gram_filled, 2 * t + h + 1)
                    for s in (0, 1):
                        last = gram_to_rows(nc.vector.tensor_copy, h, s)
                    last.then_inc(gram_copied_dve, 1)
                    if (t, h) == (0, 1):
                        dve.wait_ge(weights1_loaded, 48)
                        nc.vector.tensor_tensor(w1_dense[:, :], w1_dense_parts[:, 0, :], w1_dense_parts[:, 1, :],
                                                ALU.add).then_inc(w1_dense_ready, 1)
                elif step[0] == "layer1" and step[2] == 1:
                    t = step[1]
                    dve.wait_ge(layer1_filled, 2 * t + 2)
                    if t >= 1:
                        dve.wait_ge(layer2_filled, 2 * t)
                    for n in (2, 3):
                        last = nc.vector.tensor_scalar(hidden1[:, n, :], layer1_psum(n),
                                                       b1_sb[:, n:n + 1], 0.0, ALU.add, ALU.max)
                    last.then_inc(hidden1_dve, 1)
                elif step[0] == "layer2":
                    t = step[1]
                    if t == 0:
                        dve.wait_ge(weights23_loaded, 48)
                    dve.wait_ge(layer2_filled, 2 * t + 2)
                    if t >= 1:
                        dve.wait_ge(y_filled, t)
                    nc.vector.tensor_scalar(hidden2[:, 1, :], layer2_bank[1][:, 0:P], b2_sb[:, 1:2], 0.0,
                                            ALU.add, ALU.max).then_inc(hidden2_dve, 1)
                elif step[0] == "layer3":
                    t = step[1]
                    dve.wait_ge(y_filled, t + 1)
                    nc.vector.tensor_copy(y_row[:, t * P:(t + 1) * P], y_psum).then_inc(y_copied, 1)


def kernel(**inputs):
    import concourse.bacc as bacc
    from concourse.bass_utils import run_bass_kernel_spmd

    pair_of = {p: n for n, p in enumerate(zip(*np.triu_indices(SLOTS, k=1)))}
    w1 = np.asarray(inputs["W_top1"])
    w_rows = [D + pair_of[tuple(sorted((SLOT_FEATURES[a], SLOT_FEATURES[b])))]
              for a, b in PAIR_ROWS]
    ids = np.asarray(inputs["ids"])
    arrays = {
        "dense": np.asarray(inputs["r_dense_features"]),
        "ids": ids,
        "onehot_ids": np.ascontiguousarray(ids.T[ONEHOT_TABLES]),
        "w_pairs": w1[w_rows],
        "w_dense": np.concatenate([w1[:D], w1[-D:]]),
        "b1": np.ascontiguousarray(np.asarray(inputs["b_top1"]).reshape(N1_BLOCKS, P).T),
        "w2": np.asarray(inputs["W_top2"]),
        "b2": np.ascontiguousarray(np.asarray(inputs["b_top2"]).reshape(N2_BLOCKS, P).T),
        "w3": np.ascontiguousarray(np.asarray(inputs["W_top3"]).reshape(N2_BLOCKS, P).T),
    }
    tables = {f"tbl_{n}": np.asarray(inputs[f"tbl_{n}"]) for n in range(TABLES)}

    nc = bacc.Bacc("TRN2", target_bir_lowering=False, num_devices=1)

    def dram(name, a):
        return nc.dram_tensor(name, a.shape, mybir.dt.from_np(a.dtype), kind="ExternalInput").ap()

    given = {name: dram(name, a) for name, a in arrays.items()}
    given["tables"] = [dram(name, a) for name, a in tables.items()]
    given["out"] = nc.dram_tensor("y", (BATCH, 1), F32, kind="ExternalOutput").ap()
    dlrm_tower(nc, **given)
    result = run_bass_kernel_spmd(nc, [{**arrays, **tables}], core_ids=[0])
    return result.results[0]["y"]
```

```python
from contextlib import ExitStack

import numpy as np

import concourse.bass as bass
from concourse import mybir

F32 = mybir.dt.float32
F32R = mybir.dt.float32r
I32 = mybir.dt.int32
ALU = mybir.AluOpType
ACT = mybir.ActivationFunctionType

P = 128
BATCH = 512
TABLES = 26
SLOTS = TABLES + 1
D = 128
TILES = BATCH // P
N1, N2 = 512, 256
N1_BLOCKS, N2_BLOCKS = N1 // P, N2 // P

ONEHOT_TABLES = [11, 13, 16, 17, 19, 20, 21, 22, 23, 24]
ONEHOT_FROM = [0] * 9 + [1]
ONEHOT_ROWS = 1000
ONEHOT_CHUNKS = 8
ONEHOT_PARTS = ONEHOT_ROWS // ONEHOT_CHUNKS
NH = len(ONEHOT_TABLES)
SLOT_FEATURES = [0] + [t + 1 for t in range(TABLES) if t not in ONEHOT_TABLES]
SLOT_FEATURES += [t + 1 for t in reversed(ONEHOT_TABLES)]
GATHERED = [SLOTS - 1 - sum(first <= t for first in ONEHOT_FROM) for t in range(TILES)]
GROUP = 4


def slot_groups(t):
    starts = list(range(1, GATHERED[t] + 1, GROUP))
    if t == TILES - 1:
        starts.append(GATHERED[t])
    return [range(a, b) for a, b in zip(starts, starts[1:] + [GATHERED[t] + 1])]


GROUPS = [slot_groups(t) for t in range(TILES)]

WARM_UP = 8

REGIONS = [(t * P, P) for t in range(TILES - 1)] + [(BATCH - P, P // 2), (BATCH - P // 2, P // 2)]
TILE_REGIONS = [[t] for t in range(TILES - 1)] + [[TILES - 1, TILES]]

QUAD = 32
QUADS = P // QUAD
HALVES = [range(0, QUAD // 2), range(QUAD // 2, QUAD)]
LAST_CUTS = [0, 16, 24, 28, 32]
GRAM_PIECES = [HALVES] * (TILES - 1) + [[range(a, b) for a, b in zip(LAST_CUTS, LAST_CUTS[1:])]]

LANES = SLOTS - 1
HALF_LANES = LANES // 2
STEPS = (SLOTS + 1) // 2
CHUNKS = 3
RUNS = STEPS // CHUNKS
PAIR_READS = [(0, RUNS, LANES, 0, CHUNKS, 0, 1),
              (RUNS * LANES, 1, HALF_LANES, 0, 2, 0, STEPS - 1),
              (RUNS * LANES, 1, HALF_LANES, 2, 1, HALF_LANES, STEPS - 1)]
PAIR_PARTS = RUNS * LANES + HALF_LANES


def pair_rows():
    place = {}
    for part, runs, lanes, chunk, chunks, i, k in PAIR_READS:
        for run, lane, c in np.ndindex(runs, lanes, chunks):
            place[(chunk + c, part + run * lanes + lane)] = \
                divmod((SLOTS + 1) * (i + lane) + k + run * chunks + c, SLOTS)
    rows = [place[(c, p)] for c in range(CHUNKS) for p in range(PAIR_PARTS)]
    assert len({frozenset(r) for r in rows}) == len(rows) == SLOTS * (SLOTS - 1) // 2
    return rows


PAIR_ROWS = pair_rows()


def sample_in_tile(s, q):
    return P // 2 * (q // (QUAD // 2)) + QUAD // 2 * s + q % (QUAD // 2)


def steps():
    def transposes(t, first=0, last=None):
        return [("transpose", t, g) for g in range(len(GROUPS[t]))[first:last]]

    def gram(t):
        return [("gram", t, piece) for piece in range(len(GRAM_PIECES[t]))]

    def layer1_dense(t):
        return [("layer1_dense", t, 0), ("layer1_dense", t, 1)]

    early = transposes(0) + transposes(1)
    everywhere = sum(first == 0 for first in ONEHOT_FROM)
    order = []
    for i in range(everywhere):
        order.append(("onehot", i))
        if i >= 1:
            order.append(early.pop(0))
    order += early[:-1] + layer1_dense(0) + gram(0)
    order += [("onehot", i) for i in range(everywhere, NH)] + early[-1:]
    order += [("keep_warm", 2), ("gram", 1, 0)] + transposes(2, 0, 2) + [("gram", 1, 1)] + transposes(2, 2)
    order += [("layer1", 0, 0), ("gram", 2, 0), ("layer1", 0, 1), ("gram", 2, 1), ("layer2", 0)]
    order += transposes(3, 0, 1) + layer1_dense(1) + [("layer1", 1, 0), ("layer3", 0), ("layer1", 1, 1)]
    order += transposes(3, 1, 3) + [("layer2", 1)] + transposes(3, 3, 4) + [("layer3", 1)] + transposes(3, 4)
    order += [("layer1_dense", 2, 0)] + gram(3)
    order += [("layer1_dense", 2, 1), ("layer1", 2, 0), ("layer1", 2, 1), ("layer2", 2)] + layer1_dense(3)
    order += [("layer3", 2), ("layer1", 3, 0), ("layer1", 3, 1), ("layer2", 3), ("layer3", 3)]
    return order


def dlrm_tower(nc, dense, ids, onehot_ids, tables, w_pairs, w_dense, b1, w2, b2, w3, out):
    order = steps()
    tables_everywhere = sum(first == 0 for first in ONEHOT_FROM)
    units = [s for s in order if s[0] in ("onehot", "transpose")]
    unit_of = {s: u for u, s in enumerate(units)}
    units_before = [sum(s in unit_of for s in order[:order.index(("gram", t, 0))]) for t in range(TILES)]
    for t, n in enumerate(units_before):
        assert all(unit_of[s] < n for s in units
                   if (ONEHOT_FROM[s[1]] if s[0] == "onehot" else s[1]) <= t)
    bank_no, turns = {}, [0, 0]
    for s in units:
        borrows = int(s[0] == "transpose" and unit_of[s] < units_before[0])
        bank_no[s] = 2 * borrows + turns[borrows] % 2
        turns[borrows] += 1

    def units_before_reuse(step):
        earlier = [u for u in range(unit_of[step]) if bank_no[units[u]] == bank_no[step]]
        return earlier[-1] + 1 if earlier else 0

    def grams_done(t, piece):
        return sum(len(pieces) for pieces in GRAM_PIECES[:t]) + piece + 1

    def region_of(t, piece):
        return TILE_REGIONS[t][GRAM_PIECES[t][piece][0] * len(TILE_REGIONS[t]) // QUAD]

    scratch = nc.dram_tensor("pair_scratch", [SLOTS * SLOTS * BATCH], F32, kind="Internal").ap()

    with ExitStack() as ctx:
        def sb(name, shape, dt=F32):
            return ctx.enter_context(nc.sbuf_tensor(name, shape, dt))

        def sem(name):
            return ctx.enter_context(nc.semaphore(name))

        emb = sb("emb", [P, BATCH, SLOTS])
        dense_sb = sb("dense_sb", [P, BATCH])
        rows = sb("rows", [P, 2, GATHERED[0], D])
        gather_ids = sb("gather_ids", [P, TILES, TABLES], I32)
        match_ids = sb("match_ids", [ONEHOT_PARTS, NH, BATCH], I32)
        RAW = 3
        table_raw = sb("table_raw", [ONEHOT_PARTS, RAW, ONEHOT_CHUNKS * D])
        table_hi = sb("table_hi", [ONEHOT_PARTS, 2, ONEHOT_CHUNKS * D], F32R)
        table_lo = sb("table_lo", [ONEHOT_PARTS, 2, ONEHOT_CHUNKS * D], F32R)
        onehot = sb("onehot", [ONEHOT_PARTS, 2, ONEHOT_CHUNKS, BATCH], F32R)
        shifted_ids = sb("shifted_ids", [ONEHOT_PARTS, 2, BATCH])
        first_row_int = sb("first_row_int", [ONEHOT_PARTS, 1], I32)
        warm_up = sb("warm_up", [ONEHOT_PARTS, 1])
        minus_first_row = sb("minus_first_row", [ONEHOT_PARTS, 1])
        identity = sb("identity", [P, P])
        gram_rows = sb("gram_rows", [SLOTS, SLOTS * P])
        pairs = sb("pairs", [PAIR_PARTS, 2, CHUNKS * P])
        w1_pairs = sb("w1_pairs", [PAIR_PARTS, CHUNKS, N1])
        w1_dense_parts = sb("w1_dense_parts", [P, 2, N1])
        w1_dense = sb("w1_dense", [P, N1])
        w2_sb = sb("w2_sb", [P, N1_BLOCKS, N2])
        w3_sb = sb("w3_sb", [P, N2_BLOCKS])
        b1_sb = sb("b1_sb", [P, N1_BLOCKS])
        b2_sb = sb("b2_sb", [P, N2_BLOCKS])
        hidden1 = sb("hidden1", [P, N1_BLOCKS, P])
        hidden2 = sb("hidden2", [P, N2_BLOCKS, P])
        y_sb = sb("y_sb", [P, TILES])

        def psum(name):
            return ctx.enter_context(nc.psum_tensor(name, [P, 512], F32))

        unit_bank = [psum(f"unit_bank{i}") for i in range(2)]
        gram_bank = [psum(f"gram_bank{i}") for i in range(2)]
        layer1_bank = [psum(f"layer1_bank{i}") for i in range(2)]
        layer2_bank = [psum(f"layer2_bank{i}") for i in range(N2_BLOCKS)]

        def region_columns(j, width):
            first, samples = REGIONS[j]
            return slice(first % P * width, (first % P + samples) * width)

        def pairs_of_chunk(t, c):
            return pairs[:, t % 2, :].rearrange("i (r c s) -> i c r s", r=len(TILE_REGIONS[t]), c=CHUNKS)[:, c]

        def layer1_psum(n):
            return layer1_bank[n // 2][:, (n % 2) * P:(n % 2 + 1) * P]

        def bank_of(step):
            return (unit_bank + gram_bank)[bank_no[step]]

        gram_piece_bank = gram_bank + unit_bank
        y_psum = layer2_bank[0][:, P:P + 1]

        ids_loaded = sem("ids_loaded")
        dense_loaded = sem("dense_loaded")
        dense_placed = sem("dense_placed")
        match_ids_loaded = [sem(f"match_ids_loaded{i}") for i in range(NH)]
        table_loaded = [sem(f"table_loaded{i}") for i in range(NH)]
        second_half_loaded = sem("second_half_loaded")
        weights1_loaded = sem("weights1_loaded")
        weights23_loaded = sem("weights23_loaded")
        identity_zeroed = sem("identity_zeroed")
        identity_ready = sem("identity_ready")
        first_row_made = sem("first_row_made")
        first_row_ready = sem("first_row_ready")
        shifted_ready = sem("shifted_ready")
        gathered = {(t, g): sem(f"gathered{t}_{g}") for t in range(TILES) for g in range(len(GROUPS[t]))}
        hi_ready = sem("hi_ready")
        lo_ready = sem("lo_ready")
        onehot_ready = sem("onehot_ready")
        w1_dense_ready = sem("w1_dense_ready")
        unit_filled = sem("unit_filled")
        unit_copied = sem("unit_copied")
        gram_filled = sem("gram_filled")
        gram_copied_act = sem("gram_copied_act")
        gram_copied_dve = sem("gram_copied_dve")
        pairs_stored = [sem(f"pairs_stored{j}") for j in range(len(REGIONS))]
        pairs_loaded = [sem(f"pairs_loaded{t}") for t in range(TILES)]
        layer1_filled = sem("layer1_filled")
        hidden1_act = sem("hidden1_act")
        hidden1_dve = sem("hidden1_dve")
        layer2_filled = sem("layer2_filled")
        hidden2_act = sem("hidden2_act")
        hidden2_dve = sem("hidden2_dve")
        y_filled = sem("y_filled")
        y_copied = sem("y_copied")
        out_stored = sem("out_stored")

        block = ctx.enter_context(nc.Block())

        def table_pieces(i):
            width = ONEHOT_CHUNKS * D
            return [slice(0, width // 2), slice(width // 2, width)] if i == 0 else [slice(0, width)]

        def load_onehot_inputs(eng, i):
            if i >= RAW:
                eng.wait_ge(lo_ready, i - RAW + 1)
            eng.dma_start(match_ids[:, i, :],
                          onehot_ids[i:i + 1, :].to_broadcast([ONEHOT_PARTS, BATCH])) \
               .then_inc(match_ids_loaded[i], 16)
            source = tables[ONEHOT_TABLES[i]].rearrange("(p c) d -> p (c d)", c=ONEHOT_CHUNKS)
            for half, loaded in zip(table_pieces(i), (table_loaded[i], second_half_loaded)):
                eng.dma_start(table_raw[:, i % RAW, half], source[:, half]).then_inc(loaded, 16)

        def store_pairs(eng, j):
            first, samples = REGIONS[j]
            region = scratch[SLOTS * SLOTS * first:SLOTS * SLOTS * (first + samples)]
            return eng.dma_start(region.rearrange("(a r) -> a r", a=SLOTS),
                                 gram_rows[:, region_columns(j, SLOTS)])

        def load_pairs(eng, t, regions, read):
            part, runs, lanes, chunk, chunks, i, k = read
            first, samples = REGIONS[regions[0]]
            row = SLOTS * SLOTS * first + ((SLOTS + 1) * i + k) * samples
            lane, piece = [(SLOTS + 1) * samples, lanes], [1, chunks * samples]
            start = region_columns(regions[0], CHUNKS).start + chunk * samples
            columns = slice(start, start + chunks * samples)
            if len(regions) == 1:
                return eng.dma_start(pairs[part:part + runs * lanes, t % 2, columns],
                                     bass.AP(scratch.tensor, row, [[chunks * samples, runs], lane, piece]))
            assert runs == 1 and len(regions) == len(TILE_REGIONS[t])
            region = [SLOTS * SLOTS * samples, len(regions)]
            return eng.dma_start(pairs[part:part + lanes, t % 2, :]
                                 .rearrange("i (r x) -> i r x", r=len(regions))[:, :, columns],
                                 bass.AP(scratch.tensor, row, [lane, region, piece]))

        @block.sync
        def _(sp):
            sp.dma_start(gather_ids[:, :, :], ids).then_inc(ids_loaded, 16)
            load_onehot_inputs(sp, 0)
            load_onehot_inputs(sp, 1)
            sp.dma_start(dense_sb[:, :], dense).then_inc(dense_loaded, 16)
            for i in range(2, NH):
                load_onehot_inputs(sp, i)
                if i == NH // 2:
                    sp.dma_start(w1_dense_parts[:, :, :], w_dense.rearrange("(a p) n -> p a n", p=P)) \
                      .then_inc(weights1_loaded, 16)
                    sp.dma_start(w1_pairs[:, :, :], w_pairs.rearrange("(c p) n -> p c n", c=CHUNKS)) \
                      .then_inc(weights1_loaded, 16)
                    sp.dma_start(b1_sb[:, :], b1).then_inc(weights1_loaded, 16)
                    sp.dma_start(w2_sb[:, :, :], w2.rearrange("(a p) n -> p a n", p=P)).then_inc(weights23_loaded, 16)
                    sp.dma_start(b2_sb[:, :], b2).then_inc(weights23_loaded, 16)
                    sp.dma_start(w3_sb[:, :], w3).then_inc(weights23_loaded, 16)
            for t in range(TILES):
                for j in TILE_REGIONS[t]:
                    pieces = [piece for piece in range(len(GRAM_PIECES[t])) if region_of(t, piece) == j]
                    sp.wait_ge(gram_copied_act, grams_done(t, pieces[-1]))
                    sp.wait_ge(gram_copied_dve, grams_done(t, pieces[-1]))
                    store_pairs(sp, j).then_inc(pairs_stored[j], 16)
                if t >= 2:
                    sp.wait_ge(layer1_filled, 2 * (t - 1))
                for j in TILE_REGIONS[t]:
                    sp.wait_ge(pairs_stored[j], 16)
                    load_pairs(sp, t, [j], PAIR_READS[0]).then_inc(pairs_loaded[t], 16)
                for read in PAIR_READS[1:]:
                    load_pairs(sp, t, TILE_REGIONS[t], read).then_inc(pairs_loaded[t], 16)
            for t in range(TILES):
                sp.wait_ge(y_copied, t + 1)
                sp.dma_start(out[t * P:(t + 1) * P, :], y_sb[:, t:t + 1]).then_inc(out_stored, 16)
            sp.wait_ge(out_stored, 16 * TILES)

        @block.gpsimd
        def _(pool):
            nc.gpsimd.iota(first_row_int[:, :], pattern=[[1, 1]], base=0,
                           channel_multiplier=-ONEHOT_CHUNKS).then_inc(first_row_made, 1)
            nc.gpsimd.memset(identity[:, :], 0.0).then_inc(identity_zeroed, 1)
            pool.wait_ge(identity_zeroed, 1)
            nc.gpsimd.affine_select(out=identity[:, :], in_=identity[:, :], compare_op=ALU.not_equal,
                                    fill=1.0, base=0, pattern=[[-1, P]], channel_multiplier=1) \
                     .then_inc(identity_ready, 1)
            pool.wait_ge(ids_loaded, 16)
            for t in range(TILES):
                for g, group in enumerate(GROUPS[t]):
                    if t >= 2:
                        earlier = [group[-1] in slots for slots in GROUPS[t - 2]].index(True)
                        pool.wait_ge(unit_filled, unit_of[("transpose", t - 2, earlier)] + 1)
                    for slot in group:
                        table = SLOT_FEATURES[slot] - 1
                        pool.indirect_dma_start(
                            rows[:, t % 2, slot - 1, :], None, tables[table],
                            bass.IndirectOffsetOnAxis(ap=gather_ids[:, t, table:table + 1], axis=0),
                        ).then_inc(gathered[(t, g)], 16)

        @block.tensor
        def _(pe):
            def keep_warm(products):
                for _ in range(products):
                    nc.tensor.matmul(layer2_bank[1][:, P:2 * P], identity[:, :], identity[:, :],
                                     start=True, stop=True)

            def fill_onehot(i):
                step = ("onehot", i)
                bank = bank_of(step)
                served = BATCH - ONEHOT_FROM[i] * P
                if units_before_reuse(step):
                    pe.wait_ge(unit_copied, units_before_reuse(step))
                for part in (table_hi, table_lo):
                    if part is table_lo:
                        pe.wait_ge(lo_ready, i + 1)
                    for c in range(ONEHOT_CHUNKS):
                        if part is table_hi:
                            if i or c == 0:
                                pe.wait_ge(hi_ready, i + 1 + (i > 0))
                            elif c == ONEHOT_CHUNKS // 2:
                                pe.wait_ge(hi_ready, 2)
                            pe.wait_ge(onehot_ready, i * ONEHOT_CHUNKS + c + 1)
                        last = nc.tensor.matmul(bank[:, 0:served], part[:, i % 2, c * D:(c + 1) * D],
                                                onehot[:, i % 2, c, 0:served],
                                                start=(c == 0 and part is table_hi),
                                                stop=(c == ONEHOT_CHUNKS - 1 and part is table_lo))
                last.then_inc(unit_filled, 1)

            def fill_transpose(t, g):
                step = ("transpose", t, g)
                bank = bank_of(step)
                if units_before_reuse(step):
                    pe.wait_ge(unit_copied, units_before_reuse(step))
                pe.wait_ge(gathered[(t, g)], 16 * len(GROUPS[t][g]))
                for n, slot in enumerate(GROUPS[t][g]):
                    last = nc.tensor.transpose(bank[:, n * P:(n + 1) * P], rows[:, t % 2, slot - 1, :],
                                               identity[:, :])
                last.then_inc(unit_filled, 1)

            def fill_gram(t, piece):
                pe.wait_ge(unit_copied, units_before[t])
                if t == 0:
                    pe.wait_ge(dense_placed, 1)
                if t >= 1 and piece < len(HALVES):
                    pe.wait_ge(gram_copied_act, grams_done(t - 1, piece))
                    pe.wait_ge(gram_copied_dve, grams_done(t - 1, piece))
                samples = GRAM_PIECES[t][piece]
                for n, q in enumerate(samples):
                    for s in range(QUADS):
                        vectors = emb[:, t * P + sample_in_tile(s, q), :]
                        last = nc.tensor.matmul(
                            gram_piece_bank[piece][QUAD * s:QUAD * s + SLOTS, n * SLOTS:(n + 1) * SLOTS],
                            vectors, vectors, start=True, stop=True)
                last.then_inc(gram_filled, 1)

            def fill_layer1_dense(t, half):
                if (t, half) == (0, 0):
                    pe.wait_ge(w1_dense_ready, 1)
                    pe.wait_ge(dense_loaded, 16)
                if t >= 1:
                    pe.wait_ge((hidden1_act, hidden1_dve)[half], t)
                for n in range(2 * half, 2 * half + 2):
                    nc.tensor.matmul(layer1_psum(n), w1_dense[:, n * P:(n + 1) * P],
                                     dense_sb[:, t * P:(t + 1) * P], start=(n % 2 == 0), stop=False,
                                     skip_group_check=True)

            def fill_layer1(t, half):
                if t == 0:
                    pe.wait_ge(weights1_loaded, 48)
                pe.wait_ge(pairs_loaded[t], 16 * (len(TILE_REGIONS[t]) + len(PAIR_READS) - 1))
                for n in range(2 * half, 2 * half + 2):
                    for c in range(CHUNKS):
                        last = nc.tensor.matmul(layer1_psum(n), w1_pairs[:, c, n * P:(n + 1) * P],
                                                pairs_of_chunk(t, c),
                                                start=False, stop=(c == CHUNKS - 1),
                                                skip_group_check=True)
                last.then_inc(layer1_filled, 1)

            def fill_layer2(t):
                if t == 0:
                    pe.wait_ge(weights23_loaded, 48)
                for pair in range(N1_BLOCKS // 2):
                    pe.wait_ge((hidden1_act, hidden1_dve)[pair], t + 1)
                    for m in range(N2_BLOCKS):
                        if t >= 1 and pair == 0:
                            pe.wait_ge((hidden2_act, hidden2_dve)[m], t)
                            if m == 0:
                                pe.wait_ge(y_copied, t)
                        for n in (2 * pair, 2 * pair + 1):
                            last = nc.tensor.matmul(layer2_bank[m][:, 0:P],
                                                    w2_sb[:, n, m * P:(m + 1) * P], hidden1[:, n, :],
                                                    start=(n == 0), stop=(n == N1_BLOCKS - 1))
                        if pair == N1_BLOCKS // 2 - 1:
                            last.then_inc(layer2_filled, 1)

            def fill_layer3(t):
                for m in range(N2_BLOCKS):
                    pe.wait_ge((hidden2_act, hidden2_dve)[m], t + 1)
                    last = nc.tensor.matmul(y_psum, hidden2[:, m, :], w3_sb[:, m:m + 1],
                                            start=(m == 0), stop=(m == N2_BLOCKS - 1))
                last.then_inc(y_filled, 1)

            pe.wait_ge(identity_ready, 1)
            keep_warm(WARM_UP)
            for step in order:
                if step[0] == "keep_warm":
                    keep_warm(step[1])
                elif step[0] == "onehot":
                    fill_onehot(step[1])
                elif step[0] == "transpose":
                    fill_transpose(step[1], step[2])
                elif step[0] == "gram":
                    fill_gram(step[1], step[2])
                elif step[0] == "layer1_dense":
                    fill_layer1_dense(step[1], step[2])
                elif step[0] == "layer1":
                    fill_layer1(step[1], step[2])
                elif step[0] == "layer2":
                    fill_layer2(step[1])
                else:
                    fill_layer3(step[1])

        def gram_to_rows(copy, t, piece, s):
            samples = GRAM_PIECES[t][piece]
            j = region_of(t, piece)
            first = t * P + sample_in_tile(s, samples[0]) - REGIONS[j][0]
            return copy(gram_rows[:, region_columns(j, SLOTS)]
                        .rearrange("a (b s) -> a b s", b=SLOTS)[:, :, first:first + len(samples)],
                        gram_piece_bank[piece][QUAD * s:QUAD * s + SLOTS, 0:len(samples) * SLOTS]
                        .rearrange("a (q b) -> a b q", b=SLOTS))

        @block.scalar
        def _(act):
            def prepare_lookup(i):
                act.wait_ge(match_ids_loaded[i], 16)
                if i >= 2:
                    act.wait_ge(onehot_ready, ONEHOT_CHUNKS * (i - 1))
                served = BATCH - ONEHOT_FROM[i] * P
                nc.scalar.activation(shifted_ids[:, i % 2, 0:served], match_ids[:, i, BATCH - served:BATCH],
                                     ACT.Identity,
                                     bias=minus_first_row[:, 0:1]).then_inc(shifted_ready, 1)
                if i >= 2:
                    act.wait_ge(unit_filled, unit_of[("onehot", i - 2)] + 1)
                for half, loaded in zip(table_pieces(i), (table_loaded[i], second_half_loaded)):
                    act.wait_ge(loaded, 16)
                    nc.scalar.copy(table_hi[:, i % 2, half], table_raw[:, i % RAW, half]).then_inc(hi_ready, 1)

            act.wait_ge(first_row_ready, 1)
            nc.scalar.activation(warm_up[:, :], minus_first_row[:, :], ACT.Identity)
            prepare_lookup(0)
            prepare_lookup(1)
            act.wait_ge(dense_loaded, 16)
            nc.scalar.copy(emb[:, :, 0], dense_sb[:, :]).then_inc(dense_placed, 1)
            for step in order:
                if step[0] in ("onehot", "transpose"):
                    u = unit_of[step]
                    act.wait_ge(unit_filled, u + 1)
                    if step[0] == "onehot":
                        i = step[1]
                        served = BATCH - ONEHOT_FROM[i] * P
                        nc.scalar.copy(emb[:, BATCH - served:BATCH, SLOTS - 1 - i],
                                       bank_of(step)[:, 0:served]).then_inc(unit_copied, 1)
                        if i + 2 < NH:
                            prepare_lookup(i + 2)
                    else:
                        _, t, g = step
                        slots = GROUPS[t][g]
                        nc.scalar.copy(
                            emb[:, t * P:(t + 1) * P, slots[0]:slots[-1] + 1].rearrange("d s n -> d n s"),
                            bank_of(step)[:, 0:len(slots) * P].rearrange("d (n s) -> d n s", s=P),
                        ).then_inc(unit_copied, 1)
                elif step[0] == "gram":
                    _, t, piece = step
                    if t >= 1:
                        act.wait_ge(pairs_stored[t - 1], 16)
                    act.wait_ge(gram_filled, grams_done(t, piece))
                    for s in (2, 3):
                        last = gram_to_rows(nc.scalar.copy, t, piece, s)
                    last.then_inc(gram_copied_act, 1)
                elif step[0] == "layer1" and step[2] == 0:
                    t = step[1]
                    act.wait_ge(layer1_filled, 2 * t + 1)
                    if t >= 1:
                        act.wait_ge(layer2_filled, 2 * t)
                    if t == 0:
                        act.wait_ge(weights1_loaded, 48)
                    for n in (0, 1):
                        last = nc.scalar.activation(hidden1[:, n, :], layer1_psum(n),
                                                    ACT.Relu, bias=b1_sb[:, n:n + 1])
                    last.then_inc(hidden1_act, 1)
                elif step[0] == "layer2":
                    t = step[1]
                    if t == 0:
                        act.wait_ge(weights23_loaded, 48)
                    act.wait_ge(layer2_filled, 2 * t + 1)
                    if t >= 1:
                        act.wait_ge(y_filled, t)
                    nc.scalar.activation(hidden2[:, 0, :], layer2_bank[0][:, 0:P], ACT.Relu,
                                         bias=b2_sb[:, 0:1]).then_inc(hidden2_act, 1)

        @block.vector
        def _(dve):
            dve.wait_ge(first_row_made, 1)
            nc.vector.tensor_copy(minus_first_row[:, :], first_row_int[:, :]).then_inc(first_row_ready, 1)
            for i in range(NH):
                dve.wait_ge(shifted_ready, i + 1)
                if i >= 2:
                    dve.wait_ge(unit_filled, unit_of[("onehot", i - 2)] + 1)
                served = BATCH - ONEHOT_FROM[i] * P
                for c in range(ONEHOT_CHUNKS):
                    nc.vector.tensor_scalar(onehot[:, i % 2, c, 0:served], shifted_ids[:, i % 2, 0:served],
                                            float(c), None, ALU.is_equal) \
                             .then_inc(onehot_ready, 1)
                dve.wait_ge(table_loaded[i], 16)
                if i == 0:
                    dve.wait_ge(second_half_loaded, 16)
                dve.wait_ge(hi_ready, i + 2)
                nc.vector.tensor_tensor(table_lo[:, i % 2, :], table_raw[:, i % RAW, :],
                                        table_hi[:, i % 2, :].bitcast(F32), ALU.subtract) \
                         .then_inc(lo_ready, 1)
                if i == tables_everywhere - 1:
                    dve.wait_ge(weights1_loaded, 48)
                    nc.vector.tensor_tensor(w1_dense[:, :], w1_dense_parts[:, 0, :], w1_dense_parts[:, 1, :],
                                            ALU.add).then_inc(w1_dense_ready, 1)
            for step in order:
                if step[0] == "gram":
                    _, t, piece = step
                    if t >= 1:
                        dve.wait_ge(pairs_stored[t - 1], 16)
                    dve.wait_ge(gram_filled, grams_done(t, piece))
                    for s in (0, 1):
                        last = gram_to_rows(nc.vector.tensor_copy, t, piece, s)
                    last.then_inc(gram_copied_dve, 1)
                elif step[0] == "layer1" and step[2] == 1:
                    t = step[1]
                    dve.wait_ge(layer1_filled, 2 * t + 2)
                    if t >= 1:
                        dve.wait_ge(layer2_filled, 2 * t)
                    for n in (2, 3):
                        last = nc.vector.tensor_scalar(hidden1[:, n, :], layer1_psum(n),
                                                       b1_sb[:, n:n + 1], 0.0, ALU.add, ALU.max)
                    last.then_inc(hidden1_dve, 1)
                elif step[0] == "layer2":
                    t = step[1]
                    if t == 0:
                        dve.wait_ge(weights23_loaded, 48)
                    dve.wait_ge(layer2_filled, 2 * t + 2)
                    if t >= 1:
                        dve.wait_ge(y_filled, t)
                    nc.vector.tensor_scalar(hidden2[:, 1, :], layer2_bank[1][:, 0:P], b2_sb[:, 1:2], 0.0,
                                            ALU.add, ALU.max).then_inc(hidden2_dve, 1)
                elif step[0] == "layer3":
                    t = step[1]
                    dve.wait_ge(y_filled, t + 1)
                    nc.vector.tensor_copy(y_sb[:, t:t + 1], y_psum).then_inc(y_copied, 1)


def kernel(**inputs):
    import concourse.bacc as bacc
    from concourse.bass_utils import run_bass_kernel_spmd

    pair_of = {p: n for n, p in enumerate(zip(*np.triu_indices(SLOTS, k=1)))}
    w1 = np.asarray(inputs["W_top1"])
    w_rows = [D + pair_of[tuple(sorted((SLOT_FEATURES[a], SLOT_FEATURES[b])))]
              for a, b in PAIR_ROWS]
    ids = np.asarray(inputs["ids"])
    arrays = {
        "dense": np.ascontiguousarray(np.asarray(inputs["r_dense_features"]).T),
        "ids": np.ascontiguousarray(ids.reshape(TILES, P, TABLES).transpose(1, 0, 2)),
        "onehot_ids": np.ascontiguousarray(ids.T[ONEHOT_TABLES]),
        "w_pairs": w1[w_rows],
        "w_dense": np.concatenate([w1[:D], w1[-D:]]),
        "b1": np.ascontiguousarray(np.asarray(inputs["b_top1"]).reshape(N1_BLOCKS, P).T),
        "w2": np.asarray(inputs["W_top2"]),
        "b2": np.ascontiguousarray(np.asarray(inputs["b_top2"]).reshape(N2_BLOCKS, P).T),
        "w3": np.ascontiguousarray(np.asarray(inputs["W_top3"]).reshape(N2_BLOCKS, P).T),
    }
    tables = {f"tbl_{n}": np.asarray(inputs[f"tbl_{n}"]) for n in range(TABLES)}

    nc = bacc.Bacc("TRN2", target_bir_lowering=False, num_devices=1)

    def dram(name, a):
        return nc.dram_tensor(name, a.shape, mybir.dt.from_np(a.dtype), kind="ExternalInput").ap()

    given = {name: dram(name, a) for name, a in arrays.items()}
    given["tables"] = [dram(name, a) for name, a in tables.items()]
    given["out"] = nc.dram_tensor("y", (BATCH, 1), F32, kind="ExternalOutput").ap()
    dlrm_tower(nc, **given)
    result = run_bass_kernel_spmd(nc, [{**arrays, **tables}], core_ids=[0])
    return result.results[0]["y"]
```
